# Optimizing a Trainium2 kernel written in Bass

```python
import numpy as np
import jax
import jax.numpy as jnp

def _softmax(x, axis=-1):
    return jax.nn.softmax(x, axis=axis)

def _gelu(x):
    return jax.nn.gelu(x, approximate=True)

def _silu(x):
    return jax.nn.silu(x)

def _sigmoid(x):
    return jax.nn.sigmoid(x)

def _layernorm(x, axis=-1, eps=1e-05):
    m = jnp.mean(x, axis=axis, keepdims=True)
    v = jnp.var(x, axis=axis, keepdims=True)
    return (x - m) / jnp.sqrt(v + eps)

def _scatter_add(tgt, idx, src, axis=0):
    return tgt.at[idx].add(src)

def _segment_sum(src, seg, n):
    return jax.ops.segment_sum(src, seg, n)
kernel_name = 'mk_gnn_preln_d2_gnn_r16_ecdaef'

def setup_inputs(seed: int=0):
    np.random.seed(seed)
    _w = jnp.asarray

    def _rec_inputs():
        import jax
        import jax.numpy as jnp
        _gk = jax.random.key(seed)
        x = -0.0003713 + 1 * jax.random.normal(jax.random.fold_in(_gk, 1), (6250, 128), jnp.float32)
        src = jax.random.randint(jax.random.fold_in(_gk, 2), (200000,), 0, 6250, jnp.int32)
        dst = jax.random.randint(jax.random.fold_in(_gk, 3), (200000,), 0, 6250, jnp.int32)
        _o = jnp.argsort(dst, stable=True)
        src = src[_o]
        dst = dst[_o]
        edge_type_4 = jax.random.randint(jax.random.fold_in(_gk, 12), (200000,), 0, 4, jnp.int32)
        node_type_3 = jax.random.randint(jax.random.fold_in(_gk, 13), (6250,), 0, 3, jnp.int32)
        return (x, src, dst, edge_type_4, node_type_3)
    x, src, dst, edge_type_4, node_type_3 = _rec_inputs()

    def _L0_gnn_setup():
        import jax, jax.numpy as jnp
        import numpy as np
        N_NODES = 6250
        N_EDGES = 100000
        D = 128

        def _sage_conv(x, src, dst, Wl, bl, Wr):
            msg = x[src]
            agg = jax.ops.segment_sum(msg, dst, num_segments=N_NODES)
            deg = jax.ops.segment_sum(jnp.ones_like(dst, dtype=x.dtype), dst, num_segments=N_NODES)
            agg = agg / jnp.maximum(deg, 1.0)[:, None]
            return agg @ Wl + bl + x @ Wr
        key = jax.random.key(seed)
        ks = jax.random.split(key, 12)
        x = jax.random.normal(ks[0], (N_NODES, D), dtype=jnp.float32)
        edge_index = jax.random.randint(ks[1], (2, N_EDGES), 0, N_NODES, dtype=jnp.int64)
        s = 1.0 / np.sqrt(D)
        params = {}
        for i in range(3):
            params[f'Wl{i}'] = jax.random.uniform(ks[2 + 3 * i], (D, D), jnp.float32, -s, s)
            params[f'bl{i}'] = jax.random.uniform(ks[3 + 3 * i], (D,), jnp.float32, -s, s)
            params[f'Wr{i}'] = jax.random.uniform(ks[4 + 3 * i], (D, D), jnp.float32, -s, s)
        return {'x': x, 'edge_index': edge_index, **params}
    _L0_gnn_all = _L0_gnn_setup()
    _L0_gnn_in = {k: v for k, v in _L0_gnn_all.items() if k in ('Wl0', 'bl0', 'Wr0', 'Wl1', 'bl1', 'Wr1', 'Wl2', 'bl2', 'Wr2')}
    del _L0_gnn_all

    def _L1_gnn_setup():
        import jax, jax.numpy as jnp
        import numpy as np
        import math
        N, E, D, T, R, H = (2500, 40000, 128, 3, 4, 8)
        DK = D // H

        def _hgt_forward(node_inp, node_type, edge_index, edge_type, Wk, bk, Wq, bq, Wv, bv, Wa, ba, rel_pri, rel_att, rel_msg, skip, ln_g, ln_b):
            n = node_inp.shape[0]
            out_dim = Wk.shape[2]
            n_heads, d_k = (rel_att.shape[1], rel_att.shape[2])
            sqrt_dk = math.sqrt(d_k)
            rng = jnp.arange(n)

            def type_proj(W, b):
                all_t = jnp.einsum('ni,tio->tno', node_inp, W) + b[:, None, :]
                return all_t[node_type, rng]
            k = type_proj(Wk, bk)
            q = type_proj(Wq, bq)
            v = type_proj(Wv, bv)
            src, dst = (edge_index[0], edge_index[1])
            q_e = q[dst].reshape(-1, n_heads, d_k)
            k_e = k[src].reshape(-1, n_heads, d_k)
            v_e = v[src].reshape(-1, n_heads, d_k)
            k_rot = jnp.zeros_like(k_e)
            msg = jnp.zeros_like(v_e)
            n_rel = rel_att.shape[0]
            for r in range(n_rel):
                m = (edge_type == r)[:, None, None]
                k_rot = k_rot + jnp.where(m, jnp.einsum('ehd,hdf->ehf', k_e, rel_att[r]), 0.0)
                msg = msg + jnp.where(m, jnp.einsum('ehd,hdf->ehf', v_e, rel_msg[r]), 0.0)
            att = (q_e * k_rot).sum(-1) * rel_pri[edge_type] / sqrt_dk
            seg_max = jax.ops.segment_max(att, dst, num_segments=n)
            seg_max = jnp.where(jnp.isfinite(seg_max), seg_max, 0.0)
            ex = jnp.exp(att - seg_max[dst])
            denom = jax.ops.segment_sum(ex, dst, num_segments=n)[dst] + 1e-16
            alpha = ex / denom
            out_e = (msg * alpha[:, :, None]).reshape(-1, out_dim)
            aggr = jax.ops.segment_sum(out_e, dst, num_segments=n)
            h = jax.nn.gelu(aggr, approximate=False)
            trans_all = jnp.einsum('no,top->tnp', h, Wa) + ba[:, None, :]
            trans = trans_all[node_type, rng]
            a = jax.nn.sigmoid(skip)[node_type][:, None]
            res = trans * a + node_inp * (1.0 - a)
            mu = res.mean(-1, keepdims=True)
            var = ((res - mu) ** 2).mean(-1, keepdims=True)
            normed = (res - mu) * jax.lax.rsqrt(var + 1e-05)
            return normed * ln_g[node_type] + ln_b[node_type]
        key = jax.random.key(seed)
        ks = jax.random.split(key, 16)
        glorot = lambda k, shape, fan: jax.random.normal(k, shape, jnp.float32) * math.sqrt(2.0 / fan)
        inp = {'node_inp': jax.random.normal(ks[0], (N, D), jnp.float32), 'node_type': jax.random.randint(ks[1], (N,), 0, T), 'edge_index': jax.random.randint(ks[2], (2, E), 0, N), 'edge_type': jax.random.randint(ks[3], (E,), 0, R), 'Wk': glorot(ks[4], (T, D, D), 2 * D), 'bk': jnp.zeros((T, D), jnp.float32), 'Wq': glorot(ks[5], (T, D, D), 2 * D), 'bq': jnp.zeros((T, D), jnp.float32), 'Wv': glorot(ks[6], (T, D, D), 2 * D), 'bv': jnp.zeros((T, D), jnp.float32), 'Wa': glorot(ks[7], (T, D, D), 2 * D), 'ba': jnp.zeros((T, D), jnp.float32), 'rel_pri': jnp.ones((R, H), jnp.float32), 'rel_att': glorot(ks[8], (R, H, DK, DK), 2 * DK), 'rel_msg': glorot(ks[9], (R, H, DK, DK), 2 * DK), 'skip': jnp.ones((T,), jnp.float32), 'ln_g': jnp.ones((T, D), jnp.float32), 'ln_b': jnp.zeros((T, D), jnp.float32)}
        return inp
    _L1_gnn_all = _L1_gnn_setup()
    _L1_gnn_in = {k: v for k, v in _L1_gnn_all.items() if k in ('Wk', 'bk', 'Wq', 'bq', 'Wv', 'bv', 'Wa', 'ba', 'rel_pri', 'rel_att', 'rel_msg', 'skip', 'ln_g', 'ln_b')}
    del _L1_gnn_all
    return {'x': x, 'src': src, 'dst': dst, 'edge_type_4': edge_type_4, 'node_type_3': node_type_3, 'L0_gnn_Wl0': _L0_gnn_in['Wl0'], 'L0_gnn_bl0': _L0_gnn_in['bl0'], 'L0_gnn_Wr0': _L0_gnn_in['Wr0'], 'L0_gnn_Wl1': _L0_gnn_in['Wl1'], 'L0_gnn_bl1': _L0_gnn_in['bl1'], 'L0_gnn_Wr1': _L0_gnn_in['Wr1'], 'L0_gnn_Wl2': _L0_gnn_in['Wl2'], 'L0_gnn_bl2': _L0_gnn_in['bl2'], 'L0_gnn_Wr2': _L0_gnn_in['Wr2'], 'L1_gnn_Wk': _L1_gnn_in['Wk'], 'L1_gnn_bk': _L1_gnn_in['bk'], 'L1_gnn_Wq': _L1_gnn_in['Wq'], 'L1_gnn_bq': _L1_gnn_in['bq'], 'L1_gnn_Wv': _L1_gnn_in['Wv'], 'L1_gnn_bv': _L1_gnn_in['bv'], 'L1_gnn_Wa': _L1_gnn_in['Wa'], 'L1_gnn_ba': _L1_gnn_in['ba'], 'L1_gnn_rel_pri': _L1_gnn_in['rel_pri'], 'L1_gnn_rel_att': _L1_gnn_in['rel_att'], 'L1_gnn_rel_msg': _L1_gnn_in['rel_msg'], 'L1_gnn_skip': _L1_gnn_in['skip'], 'L1_gnn_ln_g': _L1_gnn_in['ln_g'], 'L1_gnn_ln_b': _L1_gnn_in['ln_b']}

def reference(x, src, dst, edge_type_4, node_type_3, L0_gnn_Wl0, L0_gnn_bl0, L0_gnn_Wr0, L0_gnn_Wl1, L0_gnn_bl1, L0_gnn_Wr1, L0_gnn_Wl2, L0_gnn_bl2, L0_gnn_Wr2, L1_gnn_Wk, L1_gnn_bk, L1_gnn_Wq, L1_gnn_bq, L1_gnn_Wv, L1_gnn_bv, L1_gnn_Wa, L1_gnn_ba, L1_gnn_rel_pri, L1_gnn_rel_att, L1_gnn_rel_msg, L1_gnn_skip, L1_gnn_ln_g, L1_gnn_ln_b):
    import jax
    import jax.numpy as jnp

    def _L0_gnn_ref(x, edge_index, Wl0, bl0, Wr0, Wl1, bl1, Wr1, Wl2, bl2, Wr2):
        import jax, jax.numpy as jnp
        import numpy as np
        N_NODES = 6250
        N_EDGES = 100000
        D = 128

        def _sage_conv(x, src, dst, Wl, bl, Wr):
            msg = x[src]
            agg = jax.ops.segment_sum(msg, dst, num_segments=N_NODES)
            deg = jax.ops.segment_sum(jnp.ones_like(dst, dtype=x.dtype), dst, num_segments=N_NODES)
            agg = agg / jnp.maximum(deg, 1.0)[:, None]
            return agg @ Wl + bl + x @ Wr
        src, dst = (edge_index[0], edge_index[1])
        h = jax.nn.relu(_sage_conv(x, src, dst, Wl0, bl0, Wr0))
        h = jax.nn.relu(_sage_conv(h, src, dst, Wl1, bl1, Wr1))
        return _sage_conv(h, src, dst, Wl2, bl2, Wr2)

    def _L1_gnn_ref(node_inp, node_type, edge_index, edge_type, Wk, bk, Wq, bq, Wv, bv, Wa, ba, rel_pri, rel_att, rel_msg, skip, ln_g, ln_b):
        import jax, jax.numpy as jnp
        import numpy as np
        import math
        N, E, D, T, R, H = (2500, 40000, 128, 3, 4, 8)
        DK = D // H

        def _hgt_forward(node_inp, node_type, edge_index, edge_type, Wk, bk, Wq, bq, Wv, bv, Wa, ba, rel_pri, rel_att, rel_msg, skip, ln_g, ln_b):
            n = node_inp.shape[0]
            out_dim = Wk.shape[2]
            n_heads, d_k = (rel_att.shape[1], rel_att.shape[2])
            sqrt_dk = math.sqrt(d_k)
            rng = jnp.arange(n)

            def type_proj(W, b):
                all_t = jnp.einsum('ni,tio->tno', node_inp, W) + b[:, None, :]
                return all_t[node_type, rng]
            k = type_proj(Wk, bk)
            q = type_proj(Wq, bq)
            v = type_proj(Wv, bv)
            src, dst = (edge_index[0], edge_index[1])
            q_e = q[dst].reshape(-1, n_heads, d_k)
            k_e = k[src].reshape(-1, n_heads, d_k)
            v_e = v[src].reshape(-1, n_heads, d_k)
            k_rot = jnp.zeros_like(k_e)
            msg = jnp.zeros_like(v_e)
            n_rel = rel_att.shape[0]
            for r in range(n_rel):
                m = (edge_type == r)[:, None, None]
                k_rot = k_rot + jnp.where(m, jnp.einsum('ehd,hdf->ehf', k_e, rel_att[r]), 0.0)
                msg = msg + jnp.where(m, jnp.einsum('ehd,hdf->ehf', v_e, rel_msg[r]), 0.0)
            att = (q_e * k_rot).sum(-1) * rel_pri[edge_type] / sqrt_dk
            seg_max = jax.ops.segment_max(att, dst, num_segments=n)
            seg_max = jnp.where(jnp.isfinite(seg_max), seg_max, 0.0)
            ex = jnp.exp(att - seg_max[dst])
            denom = jax.ops.segment_sum(ex, dst, num_segments=n)[dst] + 1e-16
            alpha = ex / denom
            out_e = (msg * alpha[:, :, None]).reshape(-1, out_dim)
            aggr = jax.ops.segment_sum(out_e, dst, num_segments=n)
            h = jax.nn.gelu(aggr, approximate=False)
            trans_all = jnp.einsum('no,top->tnp', h, Wa) + ba[:, None, :]
            trans = trans_all[node_type, rng]
            a = jax.nn.sigmoid(skip)[node_type][:, None]
            res = trans * a + node_inp * (1.0 - a)
            mu = res.mean(-1, keepdims=True)
            var = ((res - mu) ** 2).mean(-1, keepdims=True)
            normed = (res - mu) * jax.lax.rsqrt(var + 1e-05)
            return normed * ln_g[node_type] + ln_b[node_type]
        return _hgt_forward(node_inp, node_type, edge_index, edge_type, Wk, bk, Wq, bq, Wv, bv, Wa, ba, rel_pri, rel_att, rel_msg, skip, ln_g, ln_b)
    edge_index = jnp.stack([src, dst])
    h = jnp.maximum(_layernorm(x, axis=-1), 0.0)
    x = x + _L0_gnn_ref(h, edge_index, L0_gnn_Wl0, L0_gnn_bl0, L0_gnn_Wr0, L0_gnn_Wl1, L0_gnn_bl1, L0_gnn_Wr1, L0_gnn_Wl2, L0_gnn_bl2, L0_gnn_Wr2)
    h = jnp.maximum(_layernorm(x, axis=-1), 0.0)
    x = x + _L1_gnn_ref(h, node_type_3, edge_index, edge_type_4, L1_gnn_Wk, L1_gnn_bk, L1_gnn_Wq, L1_gnn_bq, L1_gnn_Wv, L1_gnn_bv, L1_gnn_Wa, L1_gnn_ba, L1_gnn_rel_pri, L1_gnn_rel_att, L1_gnn_rel_msg, L1_gnn_skip, L1_gnn_ln_g, L1_gnn_ln_b)
    return x

_drawn_inputs = setup_inputs


def setup_inputs(seed=0):
    import zlib

    import numpy as np

    out = dict(_drawn_inputs(seed))
    spreads = {'L1_gnn_bk': (0.0, 0.447),
     'L1_gnn_bq': (0.0, 0.555),
     'L1_gnn_bv': (0.0, 0.1),
     'L1_gnn_ba': (0.0, 0.1),
     'L1_gnn_rel_pri': (1.0, 0.2),
     'L1_gnn_skip': (1.0, 0.2),
     'L1_gnn_ln_g': (1.0, 0.2),
     'L1_gnn_ln_b': (0.0, 0.1)}
    factors = {'L0_gnn_bl0': 4.35}
    for name, (base, spread) in spreads.items():
        noise = np.random.default_rng([zlib.crc32(name.encode()), seed]).standard_normal(out[name].shape)
        drawn = base * np.exp(spread * noise) if base else spread * noise
        out[name] = jnp.asarray(drawn.astype(out[name].dtype))
    for name, factor in factors.items():
        out[name] = (out[name] * factor).astype(out[name].dtype)
    return out
```

```python
import concourse.bass as bass
from concourse import mybir
from contextlib import ExitStack


def gnn_kernel(nc, a, out):
    f32, i32, u32, bf16 = mybir.dt.float32, mybir.dt.int32, mybir.dt.uint32, mybir.dt.bfloat16
    ALU = mybir.AluOpType
    ACT = mybir.ActivationFunctionType
    AX = mybir.AxisListType

    P = 128
    N, D = a["x"].shape
    E = a["src"].shape[0]
    TYPES = a["L1_gnn_Wk"].shape[0]
    RELS, HEADS, DK, _ = a["L1_gnn_rel_att"].shape
    EPS = 1e-5
    WINDOWS = -(-N // P)
    TAIL = N - (WINDOWS - 1) * P
    CHUNKS = -(-E // P)
    WHOLE = E // P
    REST = E - WHOLE * P
    GROUP = 4
    SLOTS = 4
    ITER = GROUP * SLOTS
    STEPS = -(-(CHUNKS + WINDOWS - 1) // ITER) * ITER
    ITERS = STEPS // ITER
    TILES = -(-STEPS // P)
    TSTEPS = TILES * P
    FAR = 1 << 20
    BIG = 1e30
    RW = D + 1
    AW = D + HEADS
    BODY = 7
    assert WINDOWS % BODY == 0 and D == P and TSTEPS > STEPS and FAR > N + P
    WB = WINDOWS // BODY
    HALVES = ((0, 4), (4, 3))
    BLKS = P // HEADS
    BLK = STEPS * P // BLKS
    BSTEPS = STEPS // BLKS
    assert STEPS % BLKS == 0

    top = ExitStack()
    sb = lambda name, shape, dt: top.enter_context(nc.sbuf_tensor(name, shape, dt))
    held = []

    def sem(name):
        held.append(nc.alloc_semaphore(name))
        return held[-1]

    def next_phase():
        nc.clear_and_free_semaphores(held)
        nc.all_engine_barrier()
        held.clear()

    dram = lambda name, shape, dt: nc.dram_tensor(name, shape, dt).ap()

    with top:
        edge_rows = dram("edge_rows", (TSTEPS, 3, P), i32)
        place_rows = dram("place_rows", (TSTEPS, P), f32)
        stream = dram("stream", (TSTEPS * P + P,), f32)
        window_row = dram("window_row", (TSTEPS,), i32)
        sage_tab = [dram(f"sage_tab{l}", (WINDOWS * P, D), f32) for l in range(3)]
        x1_rows = dram("x1_rows", (WINDOWS * P, D), f32)
        hin_rows = dram("hin_rows", (WINDOWS * P, D), f32)
        kv_tab = dram("kv_tab", (WINDOWS * P * RELS, 2 * D), f32)
        v_rows = dram("v_rows", (P, STEPS, D), f32)
        join_rows = dram("join_rows", (3, TSTEPS), f32)

        iota_row = sb("iota_row", [P, P], f32)
        iota_col = sb("iota_col", [P, 1], f32)
        ident = sb("ident", [P, P], f32)
        place_T = sb("place_T", [P, TSTEPS], f32)
        src_T = sb("src_T", [P, TSTEPS], f32)
        srctype_T = sb("srctype_T", [P, TSTEPS], f32)
        window_of = sb("window_of", [1, STEPS], i32)
        idx = sb("idx", [P, SLOTS, GROUP], u32)
        ring_mem = sb("ring_mem", [P, ITER * 2 * D], f32)
        onehot = sb("onehot", [P, 2, GROUP, P], f32)
        acc_mem = sb("acc_mem", [P, WINDOWS * AW], f32)
        wide_mem = sb("wide_mem", [P, max(2 * WINDOWS * D, BLK + 2)], f32)
        att_mem = sb("att_mem", [P, STEPS * HEADS], f32)
        reset = sb("reset", [P, BLK + 2], bf16)
        work_mem = sb("work_mem", [P, (1 + SLOTS * GROUP) * P], f32)
        ones = work_mem[:, 0:P]
        psum = top.enter_context(nc.psum_tensor("psum", [P, 4096], f32))

        def carver(region, start=0):
            at = [start]

            def carve(columns, rows=P):
                at[0] += columns
                assert at[0] <= region.shape[1]
                return region[0:rows, at[0] - columns:at[0]]
            return carve

        m_pool, m_act, m_pe, m_dve = (top.enter_context(nc.semaphore(f"waited_{e}"))
                                      for e in ("pool", "act", "pe", "dve"))
        acc = acc_mem[:, :].rearrange("p (w c) -> p w c", c=AW)
        xs = att_mem[:, 0:WINDOWS * D].rearrange("p (w d) -> p w d", d=D)
        hT = wide_mem[:, 0:WINDOWS * D].rearrange("p (w d) -> p w d", d=D)
        hrow = wide_mem[:, WINDOWS * D:2 * WINDOWS * D].rearrange("p (w d) -> p w d", d=D)
        sage_ring = ring_mem[:, 0:ITER * RW].rearrange("p (s c) -> p s c", c=RW)

        def bank(i, n=1):
            return psum[:, 512 * i:512 * (i + n)]

        def windows(array, first, n):
            return array[:, bass.ds(first, n), :].rearrange("p w d -> p (w d)")

        def after(eng, semaphore, value, mark):
            eng.wait_ge(semaphore, value)
            eng.sem_inc(mark, 1)

        def load_rows(eng, m):
            _, values = nc.values_load_multi_w_load_instructions(
                window_of[0:1, bass.ds(m * GROUP, GROUP)], engines=(eng.engine,), min_val=0,
                max_val=(WINDOWS - 1) * AW,
                skip_runtime_bounds_check_because="a window is a count of WINDOWS - 1 comparisons, whatever dst is")
            return values

        pads = att_mem[:, 0:2 * P].bitcast(i32)
        last_dst_i = att_mem[:, 256:256 + TILES].bitcast(i32)
        last_dst = att_mem[:, 288:288 + TILES]
        limit = att_mem[:, 320:320 + WINDOWS - 1]
        turn = att_mem[:, 384:384 + WINDOWS - 1]
        below = att_mem[:, 448:448 + WINDOWS - 1]
        step_no = att_mem[:, 512:512 + TILES]
        win_no = att_mem[:, 544:544 + TILES]
        win_no_i = att_mem[:, 576:576 + TILES].bitcast(i32)
        win_base = att_mem[:, 608:608 + TILES]
        chunk_no = att_mem[:, 640:640 + TILES].bitcast(u32)
        compare = att_mem[:, 1024:1024 + TILES * (WINDOWS - 1)]
        edges_i = att_mem[:, 2048:2048 + TILES * 3 * P].rearrange("p (t a e) -> p t a e", a=3, e=P).bitcast(i32)
        dst_f = wide_mem[:, 0:TILES * P].rearrange("p (t e) -> p t e", e=P)
        src_f = wide_mem[:, 2048:2048 + TILES * P].rearrange("p (t e) -> p t e", e=P)
        st_f = wide_mem[:, 4096:4096 + TILES * P].rearrange("p (t e) -> p t e", e=P)
        place_f = wide_mem[:, 6144:6144 + TILES * P].rearrange("p (t e) -> p t e", e=P)

        tabs_chain = sem("tabs_chain")
        consts, padded, pads_set = sem("consts"), sem("padded"), sem("pads_set")
        last_in, tabs, counted, chunk_ready = sem("last_in"), sem("tabs"), sem("counted"), sem("chunk_ready")
        edges_in = sem("edges_in")
        tables_f, turned_over, copied = sem("tables_f"), sem("turned_over"), sem("copied")
        written, window_in = sem("written"), sem("window_in")
        sources = (a["dst"], a["src"], a["edge_type_4"])
        with nc.Block() as block:
            @block.gpsimd
            def _(pool):
                nc.gpsimd.iota(iota_row[:, :], [[1, P]], base=0, channel_multiplier=0,
                               allow_small_or_imprecise_dtypes=True).then_inc(consts, 1)
                nc.gpsimd.iota(iota_col[:, :], [[0, 1]], base=0, channel_multiplier=1,
                               allow_small_or_imprecise_dtypes=True).then_inc(consts, 1)
                nc.gpsimd.iota(step_no, [[P, TILES]], base=0, channel_multiplier=1,
                               allow_small_or_imprecise_dtypes=True).then_inc(consts, 1)
                nc.gpsimd.iota(limit, [[P, WINDOWS - 1]], base=P, channel_multiplier=0,
                               allow_small_or_imprecise_dtypes=True).then_inc(consts, 1)
                pool.wait_ge(chunk_ready, 1)
                for t in range(TILES):
                    nc.gpsimd.indirect_dma_start(
                        edges_i[:, t, :, :].rearrange("p a e -> p (a e)"), None,
                        edge_rows.rearrange("c a e -> c (a e)"),
                        bass.IndirectOffsetOnAxis(ap=chunk_no[:, t:t + 1], axis=0)).then_inc(edges_in, 16)

            @block.sync
            def _(sp):
                for n, source in enumerate(sources):
                    sp.dma_start(edge_rows[0:WHOLE, n, :], source[0:WHOLE * P].rearrange("(c e) -> c e", e=P)
                                 ).then_inc(padded, 16)
                    sp.dma_start(edge_rows[WHOLE:WHOLE + 1, n, 0:REST],
                                 source[WHOLE * P:E].rearrange("(c e) -> c e", c=1)).then_inc(padded, 16)
                sp.wait_ge(pads_set, 1)
                for n in range(3):
                    pad = pads[:, 0:P] if n == 0 else pads[:, P:2 * P]
                    sp.dma_start(edge_rows[WHOLE:WHOLE + 1, n, REST:P], pad[0:1, REST:P]).then_inc(padded, 16)
                    sp.dma_start(edge_rows[WHOLE + 1:TSTEPS, n, :], pad[0:TSTEPS - WHOLE - 1, :]
                                 ).then_inc(padded, 16)
                sp.wait_ge(padded, 12 * 16)
                sp.dma_start(last_dst_i, edge_rows[:, 0, P - 1:P].rearrange("(t p) e -> p (t e)", p=P),
                             allow_slow_non_contiguous=True).then_inc(last_in, 16)
                sp.wait_ge(tabs, 1)
                sp.dma_start(window_row.rearrange("(t p) -> p t", p=P), win_no_i,
                             allow_slow_non_contiguous=True).then_inc(written, 16)
                sp.wait_ge(tables_f, 1)
                sp.dma_start(stream[P:P + TSTEPS * P].rearrange("(t p e) -> p t e", p=P, e=P), dst_f
                             ).then_inc(written, 16)
                sp.dma_start(stream[0:P].rearrange("(c e) -> c e", c=1), ones[0:1, :]).then_inc(written, 16)
                sp.dma_start(place_rows.rearrange("(t p) e -> p t e", p=P), place_f).then_inc(written, 16)
                sp.wait_ge(written, 4 * 16)
                sp.dma_start(window_of[:, :], window_row[0:STEPS].rearrange("(a s) -> a s", a=1)).then_inc(window_in, 16)
                sp.wait_ge(window_in, 16)

            @block.vector
            def _(dve):
                did = [0]

                def step(ins):
                    did[0] += 1
                    ins.then_inc(tabs_chain, 1)
                    dve.wait_ge(tabs_chain, did[0])

                nc.vector.memset(pads[:, 0:P], FAR)
                nc.vector.memset(pads[:, P:2 * P], 0).then_inc(pads_set, 1)
                nc.vector.memset(ring_mem[:, :], 1.0)
                step(nc.vector.memset(ones[:, :], 1.0))
                dve.wait_ge(consts, 4)
                step(nc.vector.tensor_scalar(ident[:, :], iota_row[:, :], iota_col[:, :], None, ALU.is_equal))
                dve.wait_ge(last_in, 16)
                step(nc.vector.tensor_copy(last_dst, last_dst_i))
                c = compare.rearrange("p (w t) -> p w t", t=TILES)
                step(nc.vector.tensor_tensor(c, last_dst.unsqueeze(1).to_broadcast([P, WINDOWS - 1, TILES]),
                                             limit.unsqueeze(2).to_broadcast([P, WINDOWS - 1, TILES]), ALU.is_lt))
                step(nc.vector.tensor_reduce(below, c, AX.X, ALU.add))
                dve.wait_ge(counted, 1)
                step(nc.vector.scalar_tensor_tensor(turn, limit, 1.0 / P, bank(0)[:, 0:WINDOWS - 1],
                                                    ALU.mult, ALU.add))
                c = compare.rearrange("p (t w) -> p t w", t=TILES)
                step(nc.vector.tensor_tensor(c, turn.unsqueeze(1).to_broadcast([P, TILES, WINDOWS - 1]),
                                             step_no.unsqueeze(2).to_broadcast([P, TILES, WINDOWS - 1]), ALU.is_le))
                step(nc.vector.tensor_reduce(win_no, c, AX.X, ALU.add))
                step(nc.vector.tensor_tensor(chunk_no, step_no, win_no, ALU.subtract))
                nc.vector.tensor_scalar(win_base, win_no, float(P), None, ALU.mult).then_inc(chunk_ready, 1)
                nc.vector.tensor_scalar(win_no_i, win_no, float(AW), None, ALU.mult).then_inc(tabs, 1)
                dve.wait_ge(chunk_ready, 1)
                dve.wait_ge(edges_in, 16 * TILES)
                nc.vector.tensor_copy(dst_f, edges_i[:, :, 0, :])
                nc.vector.tensor_copy(src_f, edges_i[:, :, 1, :])
                step(nc.vector.tensor_copy(st_f, edges_i[:, :, 2, :]))
                nc.vector.tensor_tensor(place_f, dst_f, win_base.unsqueeze(2).to_broadcast([P, TILES, P]),
                                        ALU.subtract)
                nc.vector.scalar_tensor_tensor(st_f, src_f, float(RELS), st_f, ALU.mult, ALU.add
                                               ).then_inc(tables_f, 1)
                for t in range(TILES):
                    for n, table in enumerate((place_T, src_T, srctype_T)):
                        j = 3 * t + n
                        dve.wait_ge(turned_over, j + 1)
                        nc.vector.tensor_copy(table[:, t * P:(t + 1) * P], bank(1 + j % 4)[:, 0:P]
                                              ).then_inc(copied, 1)

            @block.tensor
            def _(pe):
                pe.wait_ge(tabs_chain, 5)
                nc.tensor.matmul(bank(0)[:, 0:WINDOWS - 1], ones[:, :], below, start=True, stop=True
                                 ).then_inc(counted, 1)
                pe.wait_ge(tables_f, 1)
                for t in range(TILES):
                    for n, table in enumerate((place_f, src_f, st_f)):
                        j = 3 * t + n
                        if j >= 4:
                            pe.wait_ge(copied, j - 3)
                        nc.tensor.transpose(bank(1 + j % 4)[:, 0:P], table[:, t, :], ident[:, :]
                                            ).then_inc(turned_over, 1)

        def norm_block(tag, table, x_source):
            carve = carver(att_mem, WINDOWS * D)
            mean, rstd = carve(WINDOWS), carve(WINDOWS)
            stage = carve(8 * P).rearrange("p (b c) -> p b c", b=2)
            x_in, chain = sem(f"x_in_{tag}"), sem(f"norm_chain_{tag}")
            squared, rooted = sem(f"squared_{tag}"), sem(f"rooted_{tag}")
            varied, h_done = sem(f"varied_{tag}"), sem(f"h_done_{tag}")
            hT_psum, hT_done, stored = sem(f"hT_psum_{tag}"), sem(f"hT_done_{tag}"), sem(f"h_stored_{tag}")
            staged, x_zero = sem(f"staged_{tag}"), sem(f"x_zero_{tag}")
            centred_sem = sem(f"centred_{tag}")
            centred = hrow
            square = hT
            bc = lambda v: v.unsqueeze(2).to_broadcast([P, WINDOWS, D])
            with nc.Block() as block:
                @block.sync
                def _(sp):
                    if x_source is not None:
                        body, tail = x_source[0:(WINDOWS - 1) * P, :], x_source[(WINDOWS - 1) * P:N, :]
                        sp.wait_ge(x_zero, 1)
                        sp.dma_start(xs[:, 0:WINDOWS - 1, :], body.rearrange("(w p) d -> p w d", p=P)
                                     ).then_inc(x_in, 16)
                        sp.dma_start(xs[0:TAIL, WINDOWS - 1, :], tail).then_inc(x_in, 16)
                    else:
                        sp.dma_start(x1_rows.rearrange("(w p) d -> p w d", p=P), xs).then_inc(x_in, 16)
                    sp.wait_ge(h_done, 1)
                    sp.dma_start(table.rearrange("(w p) d -> p w d", p=P), hrow).then_inc(stored, 16)
                    sp.wait_ge(stored, 16)
                    sp.wait_ge(x_in, 32 if x_source is not None else 16)

                @block.vector
                def _(dve):
                    if x_source is not None:
                        nc.vector.memset(xs[:, WINDOWS - 1, :], 0.0).then_inc(x_zero, 1)
                        dve.wait_ge(x_in, 32)
                    nc.vector.tensor_reduce(mean, xs, AX.X, ALU.add).then_inc(chain, 1)
                    dve.wait_ge(chain, 1)
                    nc.vector.tensor_scalar(mean, mean, 1.0 / D, None, ALU.mult).then_inc(chain, 1)
                    dve.wait_ge(chain, 2)
                    nc.vector.tensor_tensor(centred, xs, bc(mean), ALU.subtract).then_inc(centred_sem, 1)
                    dve.wait_ge(squared, 1)
                    nc.vector.tensor_reduce(rstd, square, AX.X, ALU.add).then_inc(chain, 1)
                    dve.wait_ge(chain, 3)
                    nc.vector.tensor_scalar(rstd, rstd, 1.0 / D, EPS, ALU.mult, ALU.add
                                            ).then_inc(varied, 1)
                    dve.wait_ge(rooted, 1)
                    nc.vector.reciprocal(rstd, rstd).then_inc(chain, 1)
                    dve.wait_ge(chain, 4)
                    nc.vector.scalar_tensor_tensor(hrow, centred, 0.0, bc(rstd), ALU.max, ALU.mult
                                                   ).then_inc(h_done, 1)
                    dve.wait_ge(h_done, 1)
                    with dve.Fori(0, WB) as i:
                        for b, (first, n) in enumerate(HALVES):
                            dve.wait_ge(hT_done, i * 2 + b + 1)
                            nc.vector.tensor_copy(stage[:, b, 0:n * P], windows(hrow, i * BODY + first, n)
                                                  ).then_inc(staged, 1)

                @block.scalar
                def _(act):
                    act.wait_ge(centred_sem, 1)
                    nc.scalar.activation(square, centred, ACT.Square).then_inc(squared, 1)
                    act.wait_ge(varied, 1)
                    nc.scalar.activation(rstd, rstd, ACT.Sqrt).then_inc(rooted, 1)
                    with act.Fori(0, WB) as i:
                        for b, (first, n) in enumerate(HALVES):
                            after(act, hT_psum, i * 2 + b + 1, m_act)
                            nc.scalar.activation(windows(hT, i * BODY + first, n), bank(b)[:, 0:n * P], ACT.Copy
                                                 ).then_inc(hT_done, 1)

                @block.tensor
                def _(pe):
                    pe.wait_ge(h_done, 1)
                    pe.sem_inc(hT_done, 2)
                    with pe.Fori(0, WB) as i:
                        for b, (first, n) in enumerate(HALVES):
                            pe.wait_ge(hT_done, i * 2 + b + 1)
                            pe.wait_ge(staged, i * 2 + b + 1)
                            for j in range(n):
                                last = nc.tensor.transpose(bank(b)[:, j * P:(j + 1) * P],
                                                           stage[:, b, j * P:(j + 1) * P], ident[:, :])
                            last.then_inc(hT_psum, 1)

        def sage_edges(l):
            idx_ready, onehot_ready = sem(f"idx_ready{l}"), sem(f"onehot_ready{l}")
            gathered = [sem(f"gathered{l}_{h}") for h in range(SLOTS)]
            groups_summed, added = sem(f"groups_summed{l}"), sem(f"added{l}")
            part = lambda m: bank(2 * (m % 2), 2).rearrange("p (u c) -> p u c", c=2 * D)
            with nc.Block() as block:
                @block.scalar
                def _(act):
                    with act.Fori(0, ITERS) as k:
                        for h in range(SLOTS):
                            m = k * SLOTS + h
                            after(act, groups_summed, m + 1, m_act)
                            nc.scalar.activation(idx[:, h, :], src_T[:, bass.ds(m * GROUP, GROUP)], ACT.Copy
                                                 ).then_inc(idx_ready, 1)

                @block.gpsimd
                def _(pool):
                    with pool.Fori(0, ITERS) as k:
                        for h in range(SLOTS):
                            after(pool, idx_ready, k * SLOTS + h + 1, m_pool)
                            for u in range(GROUP):
                                nc.gpsimd.indirect_dma_start(
                                    sage_ring[:, h * GROUP + u, 0:D], None, sage_tab[l],
                                    bass.IndirectOffsetOnAxis(ap=idx[:, h, u:u + 1], axis=0)
                                ).then_inc(gathered[h], 16)

                @block.tensor
                def _(pe):
                    pe.sem_inc(groups_summed, SLOTS)
                    with pe.Fori(0, ITERS) as k:
                        for h in range(SLOTS):
                            m = k * SLOTS + h
                            pe.wait_ge(onehot_ready, m + 1)
                            pe.wait_ge(added, m * GROUP + GROUP)
                            pe.wait_ge(gathered[h], (k + 1) * (16 * GROUP))
                            for u in range(GROUP):
                                last = nc.tensor.matmul(part(h)[:, u, 0:RW], onehot[:, h % 2, u, :],
                                                        sage_ring[:, h * GROUP + u, :], start=True, stop=True)
                            last.then_inc(groups_summed, 1)

                @block.vector
                def _(dve):
                    def make_onehot(m, h):
                        nc.vector.tensor_tensor(
                            onehot[:, h % 2, :, :],
                            place_T[:, bass.ds(m * GROUP, GROUP)].unsqueeze(2).to_broadcast([P, GROUP, P]),
                            iota_row[:, :].unsqueeze(1).to_broadcast([P, GROUP, P]),
                            ALU.is_equal).then_inc(onehot_ready, 1)

                    dve.sem_inc(added, 2 * GROUP - 1)
                    nc.vector.memset(acc_mem[:, :], 0.0).then_inc(added, 1)
                    make_onehot(0, 0)
                    with dve.Fori(0, ITERS) as k:
                        for h in range(SLOTS):
                            m = k * SLOTS + h
                            dve.wait_ge(groups_summed, m + SLOTS)
                            make_onehot(m + 1, h + 1)
                            dve.wait_ge(groups_summed, m + 1 + SLOTS)
                            for u, at in enumerate(load_rows(dve, m)):
                                s = m * GROUP + u
                                row = acc_mem[:, bass.ds(at, RW)]
                                dve.wait_ge(added, s + 2 * GROUP)
                                nc.vector.tensor_tensor(row, row, part(h)[:, u, 0:RW], ALU.add
                                                        ).then_inc(added, 1)

        def sage_nodes(l, Wl, bl, Wr):
            last_layer = l == 2
            carve = carver(att_mem, WINDOWS * D)
            wl, wr, bcol, rdeg = carve(D), carve(D), carve(1), carve(WINDOWS)
            mean_rows, meanT, convT = (carve(8 * P).rearrange("p (b c) -> p b c", b=2) for _ in range(3))
            w_in, chain = sem(f"w_in{l}"), sem(f"mean_chain{l}")
            mean_ready, mean_turned, meanT_ready = sem(f"mean_ready{l}"), sem(f"mean_turned{l}"), sem(f"meanT_ready{l}")
            conv_done, convT_ready, hT_kept = sem(f"conv_done{l}"), sem(f"convT_ready{l}"), sem(f"hT_kept{l}")
            conv_turned, rows, stored = sem(f"conv_turned{l}"), sem(f"rows{l}"), sem(f"rows_stored{l}")
            rows_out = None if last_layer else sage_tab[l + 1].rearrange("(w p) d -> p w d", p=P)
            with nc.Block() as block:
                @block.sync
                def _(sp):
                    sp.dma_start(wl, Wl).then_inc(w_in, 16)
                    sp.dma_start(wr, Wr).then_inc(w_in, 16)
                    sp.dma_start(bcol, bl.rearrange("(d o) -> d o", o=1),
                                 allow_slow_non_contiguous=True).then_inc(w_in, 16)
                    if not last_layer:
                        with sp.Fori(0, WB) as i:
                            sp.wait_ge(rows, (i + 2) * 2)
                            sp.dma_start(rows_out[:, bass.ds(i * BODY, BODY), :],
                                         hrow[:, bass.ds(i * BODY, BODY), :]).then_inc(stored, 16)
                        sp.wait_ge(stored, 16 * WB)

                @block.vector
                def _(dve):
                    def make_means(i):
                        for b, (first, n) in enumerate(HALVES):
                            dve.wait_ge(mean_turned, i * 2 + b + 1)
                            nc.vector.tensor_tensor(
                                mean_rows[:, b, 0:n * P].rearrange("p (w d) -> p w d", d=D),
                                acc[:, bass.ds(i * BODY + first, n), 0:D],
                                rdeg[:, bass.ds(i * BODY + first, n)].unsqueeze(2).to_broadcast([P, n, D]),
                                ALU.mult).then_inc(mean_ready, 1)

                    def take_rows(i):
                        for b, (first, n) in enumerate(HALVES):
                            dve.wait_ge(conv_turned, i * 2 + b + 3)
                            if last_layer:
                                row = windows(xs, i * BODY + first, n)
                                nc.vector.tensor_tensor(row, row, bank(4 + b)[:, 0:n * P], ALU.add
                                                        ).then_inc(rows, 1)
                            else:
                                nc.vector.tensor_copy(windows(hrow, i * BODY + first, n),
                                                      bank(4 + b)[:, 0:n * P]).then_inc(rows, 1)

                    deg = acc[:, :, D:D + 1].rearrange("p w o -> p (w o)")
                    nc.vector.tensor_scalar(rdeg, deg, 1.0, None, ALU.max).then_inc(chain, 1)
                    dve.wait_ge(chain, 1)
                    nc.vector.reciprocal(rdeg, rdeg).then_inc(chain, 1)
                    dve.wait_ge(chain, 2)
                    dve.sem_inc(mean_turned, 2)
                    make_means(0)
                    with dve.Fori(0, WB - 1) as i:
                        make_means(i + 1)
                        take_rows(i)
                    take_rows(WB - 1)

                @block.scalar
                def _(act):
                    def copy_means(i):
                        for b, (first, n) in enumerate(HALVES):
                            act.wait_ge(mean_turned, i * 2 + b + 3)
                            nc.scalar.activation(meanT[:, b, 0:n * P], bank(b)[:, 0:n * P], ACT.Copy
                                                 ).then_inc(meanT_ready, 1)

                    def take_convs(i):
                        way = ACT.Identity if last_layer else ACT.Relu
                        for b, (first, n) in enumerate(HALVES):
                            act.wait_ge(conv_turned, i * 2 + b + 1)
                            act.wait_ge(conv_done, i * 2 + b + 1)
                            nc.scalar.activation(convT[:, b, 0:n * P], bank(2 + b)[:, 0:n * P], way, bias=bcol
                                                 ).then_inc(convT_ready, 1)
                            if not last_layer:
                                nc.scalar.activation(windows(hT, i * BODY + first, n), bank(2 + b)[:, 0:n * P],
                                                     way, bias=bcol).then_inc(hT_kept, 1)

                    act.sem_inc(conv_turned, 2)
                    act.wait_ge(w_in, 48)
                    copy_means(0)
                    with act.Fori(0, WB - 1) as i:
                        take_convs(i)
                        copy_means(i + 1)
                    take_convs(WB - 1)

                @block.tensor
                def _(pe):
                    def turn_means(i):
                        for b, (first, n) in enumerate(HALVES):
                            pe.wait_ge(meanT_ready, i * 2 + b + 1)
                            pe.wait_ge(mean_ready, i * 2 + b + 1)
                            for j in range(n):
                                last = nc.tensor.transpose(bank(b)[:, j * P:(j + 1) * P],
                                                           mean_rows[:, b, j * P:(j + 1) * P], ident[:, :])
                            last.then_inc(mean_turned, 1)

                    def convolve(i):
                        bank_read = convT_ready if last_layer else hT_kept
                        for b, (first, n) in enumerate(HALVES):
                            pe.wait_ge(meanT_ready, i * 2 + b + 3)
                            pe.wait_ge(bank_read, i * 2 + b + 1)
                            nc.tensor.matmul(bank(2 + b)[:, 0:n * P], wl, meanT[:, b, 0:n * P],
                                             start=True, stop=False)
                            nc.tensor.matmul(bank(2 + b)[:, 0:n * P], wr,
                                             windows(hT, i * BODY + first, n), start=False, stop=True
                                             ).then_inc(conv_done, 1)

                    def turn_back(i):
                        for b, (first, n) in enumerate(HALVES):
                            pe.wait_ge(rows, i * 2 + b + 1)
                            pe.wait_ge(convT_ready, i * 2 + b + ready_from)
                            for j in range(n):
                                last = nc.tensor.transpose(bank(4 + b)[:, j * P:(j + 1) * P],
                                                           convT[:, b, j * P:(j + 1) * P], ident[:, :])
                            last.then_inc(conv_turned, 1)

                    pe.wait_ge(w_in, 48)
                    pe.sem_inc(rows, 2)
                    pe.sem_inc(meanT_ready, 2)
                    pe.sem_inc(convT_ready if last_layer else hT_kept, 2)
                    ready_from = 3 if last_layer else 1
                    turn_means(0)
                    with pe.Fori(0, WB - 1) as i:
                        convolve(i)
                        turn_means(i + 1)
                        turn_back(i)
                    convolve(WB - 1)
                    turn_back(WB - 1)

        next_phase()
        norm_block("a", sage_tab[0], a["x"])
        next_phase()
        for l in range(3):
            sage_edges(l)
            sage_nodes(l, a[f"L0_gnn_Wl{l}"], a[f"L0_gnn_bl{l}"], a[f"L0_gnn_Wr{l}"])
            next_phase()

        norm_block("b", hin_rows, None)
        next_phase()
        SCALE = float(DK) ** -0.5
        q_all = acc[:, :, 0:D]
        kv_ring = ring_mem[:, :].rearrange("p (s c) -> p s c", c=2 * D)

        types_bc = hrow.rearrange("p w d -> p (w d)")
        types_bi = types_bc.bitcast(i32)
        carve = carver(att_mem)
        w_kqv = carve(9 * D).rearrange("p (n t o) -> p n t o", n=3, t=TYPES)
        b_kqv = carve(3 * D, TYPES).rearrange("p (n o) -> p n o", n=3)
        rotate = carve(2 * RELS * D).rearrange("p (n c) -> p n c", n=2)
        pri_bc = carve(RELS * HEADS)
        hT_typed = carve(2 * TYPES * 4 * P).rearrange("p (b t c) -> p b t c", b=2, t=TYPES)
        is_type = carve(2 * 4 * P, TYPES).rearrange("p (b c) -> p b c", b=2)
        kvT = carve(4 * 4 * P).rearrange("p (b n c) -> p b n c", b=2, n=2)
        kv_spare = carve(3 * RELS * 2 * D)
        kv_rows = [ring_mem[:, j * 1024:(j + 1) * 1024] if j < 4 else kv_spare[:, (j - 4) * 1024:(j - 3) * 1024]
                   for j in range(BODY)]
        assert RELS * 2 * D == 1024
        w_in, bd_zero, bd_in = sem("hgt_w_in"), sem("bd_zero"), sem("bd_in")
        types_in, types_end, types_f = sem("types_in"), sem("types_end"), sem("types_f")
        rotate_ready, typed = sem("rotate_ready"), sem("typed")
        kvT_psum, kT_copied, vT_copied, q_psum, q_copied = (sem("kvT_psum"), sem("kT_copied"), sem("vT_copied"),
                                                            sem("q_psum"), sem("q_copied"))
        kv_psum, k_copied, v_copied, kv_free = sem("kv_psum"), sem("k_copied"), sem("v_copied"), sem("kv_free")
        kv_stored = [sem(f"kv_stored{j}") for j in range(BODY)]
        kv_tab_w = kv_tab.rearrange("(w p r) c -> p w (r c)", p=P, r=RELS)
        with nc.Block() as block:
            @block.sync
            def _(sp):
                for n, name in enumerate(("k", "v", "q")):
                    sp.dma_start(w_kqv[:, n, :, :], a[f"L1_gnn_W{name}"].rearrange("t i o -> i t o")
                                 ).then_inc(w_in, 16)
                    sp.dma_start(b_kqv[:, n, :], a[f"L1_gnn_b{name}"]).then_inc(w_in, 16)
                sp.dma_start(pri_bc, a["L1_gnn_rel_pri"].rearrange("r h -> (r h)").partition_broadcast(P)
                             ).then_inc(w_in, 16)
                sp.dma_start(types_bi[:, 0:N], a["node_type_3"].partition_broadcast(P)).then_inc(types_in, 16)
                sp.wait_ge(bd_zero, 1)
                for n, name in enumerate(("att", "msg")):
                    for hd in range(HEADS):
                        at = slice(hd * DK, (hd + 1) * DK)
                        sp.dma_start(rotate[at, n, :].rearrange("p (r f) -> p r f", r=RELS)[:, :, at],
                                     a[f"L1_gnn_rel_{name}"][:, hd, :, :].rearrange("r d f -> d r f")
                                     ).then_inc(bd_in, 16)
                with sp.Fori(0, WB) as i:
                    for j in range(BODY):
                        sp.wait_ge(k_copied, i * BODY + j + 3)
                        sp.wait_ge(v_copied, i * BODY + j + 3)
                        sp.dma_start(kv_tab_w[:, bass.ds(i * BODY + j, 1), :].rearrange("p w c -> p (w c)"),
                                     kv_rows[j]).then_inc(kv_stored[j], 16)
                        if j >= 3:
                            sp.wait_ge(kv_stored[j - 3], (i + 1) * 16)
                            sp.sem_inc(kv_free, 1)
                    for j in range(BODY - 3, BODY):
                        sp.wait_ge(kv_stored[j], (i + 1) * 16)
                        sp.sem_inc(kv_free, 1)

            @block.vector
            def _(dve):
                nc.vector.memset(rotate, 0.0).then_inc(bd_zero, 1)
                nc.vector.memset(types_bi[:, N:WINDOWS * P], 0).then_inc(types_end, 1)
                dve.wait_ge(types_in, 16)
                dve.wait_ge(types_end, 1)
                nc.vector.tensor_copy(types_bc, types_bi).then_inc(types_f, 1)
                dve.wait_ge(bd_in, 32 * HEADS)
                dve.wait_ge(w_in, 7 * 16)
                pri = rotate[:, 0, :].rearrange("p (g f) -> p g f", f=DK)
                nc.vector.scalar_tensor_tensor(pri, pri, SCALE, pri_bc.unsqueeze(2).to_broadcast(
                    [P, RELS * HEADS, DK]), ALU.mult, ALU.mult).then_inc(rotate_ready, 1)
                dve.wait_ge(types_f, 1)

                def type_halves(q, w, b, n):
                    dve.wait_ge(q_psum, q + 1)
                    for t in range(TYPES):
                        nc.vector.scalar_tensor_tensor(
                            hT_typed[:, b, t, 0:n * P], types_bc[:, bass.ds(w * P, n * P)], float(t),
                            windows(hT, w, n), ALU.is_equal, ALU.mult)
                    nc.vector.tensor_scalar(is_type[:, b, 0:n * P], types_bc[0:TYPES, bass.ds(w * P, n * P)],
                                            iota_col[0:TYPES, :], None, ALU.is_equal).then_inc(typed, 1)

                dve.sem_inc(q_psum, 2)
                dve.sem_inc(v_copied, 2)
                with dve.Fori(0, WB) as i:
                    for b, (first, n) in enumerate(HALVES):
                        type_halves(i * 2 + b, i * BODY + first, b, n)
                    for b, (first, n) in enumerate(HALVES):
                        q = i * 2 + b
                        dve.wait_ge(kvT_psum, q + 1)
                        nc.vector.tensor_copy(kvT[:, b, 1, 0:n * P], bank(1)[:, 0:n * P]).then_inc(vT_copied, 1)
                        dve.wait_ge(q_psum, q + 3)
                        nc.vector.tensor_copy(q_all[:, bass.ds(i * BODY + first, n), :],
                                              bank(2)[:, 0:n * P].rearrange("p (w d) -> p w d", d=D)
                                              ).then_inc(q_copied, 1)
                        for j in range(first, first + n):
                            w = i * BODY + j
                            dve.wait_ge(kv_free, w + 1)
                            dve.wait_ge(kv_psum, w + 1)
                            nc.vector.tensor_copy(kv_rows[j].rearrange("p (r c) -> p r c", r=RELS)[:, :, D:2 * D],
                                                  bank(4 + 2 * (j % 2)).rearrange("p (r d) -> p r d", r=RELS)
                                                  ).then_inc(v_copied, 1)

            @block.scalar
            def _(act):
                act.sem_inc(kv_free, BODY)
                act.sem_inc(k_copied, 2)
                with act.Fori(0, WB) as i:
                    for b, (first, n) in enumerate(HALVES):
                        q = i * 2 + b
                        act.wait_ge(kvT_psum, q + 1)
                        nc.scalar.activation(kvT[:, b, 0, 0:n * P], bank(0)[:, 0:n * P], ACT.Copy
                                             ).then_inc(kT_copied, 1)
                        for j in range(first, first + n):
                            w = i * BODY + j
                            act.wait_ge(kv_free, w + 1)
                            act.wait_ge(kv_psum, w + 1)
                            nc.scalar.activation(kv_rows[j].rearrange("p (r c) -> p r c", r=RELS)[:, :, 0:D],
                                                 bank(3 + 2 * (j % 2)).rearrange("p (r d) -> p r d", r=RELS),
                                                 ACT.Copy).then_inc(k_copied, 1)

            @block.tensor
            def _(pe):
                pe.wait_ge(w_in, 7 * 16)
                pe.wait_ge(rotate_ready, 1)
                pe.sem_inc(q_copied, 1)
                with pe.Fori(0, WB) as i:
                    for b, (first, n) in enumerate(HALVES):
                        q = i * 2 + b
                        pe.wait_ge(typed, q + 1)
                        for m in range(2):
                            for t in range(TYPES):
                                nc.tensor.matmul(bank(m)[:, 0:n * P], w_kqv[:, m, t, :], hT_typed[:, b, t, 0:n * P],
                                                 start=(t == 0), stop=False)
                            last = nc.tensor.matmul(bank(m)[:, 0:n * P], b_kqv[:, m, :], is_type[:, b, 0:n * P],
                                                    start=False, stop=True)
                        last.then_inc(kvT_psum, 1)
                        pe.wait_ge(q_copied, q + 1)
                        for j in range(n):
                            at = slice(j * P, (j + 1) * P)
                            for t in range(TYPES):
                                nc.tensor.matmul(bank(2)[:, at], hT_typed[:, b, t, at], w_kqv[:, 2, t, :],
                                                 start=(t == 0), stop=False)
                            last = nc.tensor.matmul(bank(2)[:, at], is_type[:, b, at], b_kqv[:, 2, :],
                                                    start=False, stop=True)
                        last.then_inc(q_psum, 1)
                        pe.wait_ge(kT_copied, q + 1)
                        pe.wait_ge(vT_copied, q + 1)
                        for j in range(first, first + n):
                            w = i * BODY + j
                            at = slice((j - first) * P, (j - first + 1) * P)
                            pe.wait_ge(k_copied, w + (2 if j == 0 else 1))
                            pe.wait_ge(v_copied, w + (2 if j == 0 else 1))
                            nc.tensor.matmul(bank(3 + 2 * (j % 2)), kvT[:, b, 0, at], rotate[:, 0, :],
                                             start=True, stop=True)
                            nc.tensor.matmul(bank(4 + 2 * (j % 2)), kvT[:, b, 1, at], rotate[:, 1, :],
                                             start=True, stop=True).then_inc(kv_psum, 1)

        next_phase()

        GH = GROUP * HEADS
        assert ITER * HEADS == P
        work = carver(work_mem)
        turn_stage = work(P)
        placeT_bc = work(SLOTS * GROUP * P).rearrange("p (h c) -> p h c", h=SLOTS)
        carve = carver(wide_mem)
        dst_rows, shut_rows = (carve(TILES * P).rearrange("p (t e) -> p t e", e=P) for _ in range(2))
        before, joins, whole, through = (carve(TILES) for _ in range(4))
        both_ways = bank(2)[:, P:2 * P]
        shut_now = bank(3)[:, 0:P + 1]
        SHUT_AT = BLK - STEPS
        shut_T = wide_mem[:, SHUT_AT:SHUT_AT + STEPS]
        assert all(P * (k + 1) <= SHUT_AT + ITER * (k + 1) for k in range(ITERS - 1)) and SHUT_AT > 4 * TILES * P
        onehotT = onehot[:, :, :, :].rearrange("p b u c -> p b (u c)")
        maxima = wide_mem[:, 0:BLK]
        outside = src_T[:, 0:STEPS]
        idx_ready, scored, v_saved, v_stored = sem("kv_idx_ready"), sem("scored"), sem("v_saved"), sem("v_stored")
        gathered = [sem(f"kv_gathered{h}") for h in range(SLOTS)]
        place_in = [sem(f"place_in{h}") for h in range(SLOTS)]
        onehotT_ready, q_ready, multiplied = sem("onehotT_ready"), sem("q_ready"), sem("multiplied")
        prep, joins_ready, joins_stored = sem("prep_scores"), sem("joins_ready"), sem("joins_stored")
        masked, stage_ready, scores_turned, run_max = sem("masked"), sem("turn_stage_ready"), sem("scores_turned"), sem("run_max")
        dst_in, rows_ready, shut_turned, shut = sem("dst_in"), sem("shut_rows"), sem("shut_turned"), sem("shut")
        shut_kept = sem("shut_kept")
        places = place_rows.rearrange("s e -> (s e)")
        stream_steps = stream[P:P + TSTEPS * P].rearrange("(s e) -> s e", e=P)
        with nc.Block() as block:
            @block.sync
            def _(sp):
                sp.dma_start(dst_rows, stream[P:P + TSTEPS * P].rearrange("(t p e) -> p t e", p=P, e=P)
                             ).then_inc(dst_in, 16)
                sp.dma_start(before, bass.AP(stream.tensor, P - 1, [[P, P], [P * P, TILES]]),
                             allow_slow_non_contiguous=True).then_inc(dst_in, 16)
                sp.sem_inc(v_saved, SLOTS)
                sp.wait_ge(joins_ready, 1)
                for n, column in enumerate((joins, whole, through)):
                    sp.dma_start(join_rows[n, :].rearrange("(t p) -> p t", p=P), column,
                                 allow_slow_non_contiguous=True).then_inc(joins_stored, 16)
                with sp.Fori(0, ITERS) as k:
                    for h in range(SLOTS):
                        m = k * SLOTS + h
                        sp.wait_ge(gathered[h], (k + 1) * (16 * GROUP))
                        sp.dma_start(v_rows[:, bass.ds(m * GROUP, GROUP), :],
                                     kv_ring[:, h * GROUP:(h + 1) * GROUP, D:2 * D]).then_inc(v_stored, 16)
                        sp.wait_ge(v_stored, (m + 1) * 16)
                        sp.sem_inc(v_saved, 1)
                sp.wait_ge(joins_stored, 48)

            @block.scalar
            def _(act):
                with act.Fori(0, ITERS) as k:
                    for h in range(SLOTS):
                        m = k * SLOTS + h
                        act.wait_ge(v_saved, m + 1)
                        after(act, scored, m + 1, m_act)
                        nc.scalar.activation(idx[:, h, :], srctype_T[:, bass.ds(m * GROUP, GROUP)], ACT.Copy
                                             ).then_inc(idx_ready, 1)
                        act.dma_start(placeT_bc[:, h, :],
                                      places[bass.ds(m * (GROUP * P), GROUP * P)].partition_broadcast(P)
                                      ).then_inc(place_in[h], 16)

            @block.gpsimd
            def _(pool):
                with pool.Fori(0, ITERS) as k:
                    for h in range(SLOTS):
                        after(pool, idx_ready, k * SLOTS + h + 1, m_pool)
                        for u in range(GROUP):
                            nc.gpsimd.indirect_dma_start(
                                kv_ring[:, h * GROUP + u, :], None, kv_tab,
                                bass.IndirectOffsetOnAxis(ap=idx[:, h, u:u + 1], axis=0)
                            ).then_inc(gathered[h], 16)

            @block.tensor
            def _(pe):
                pe.wait_ge(rows_ready, 1)
                for t in range(TILES):
                    if t >= 4:
                        pe.wait_ge(shut_kept, t - 3)
                    nc.tensor.transpose(bank(4 + t % 4)[:, 0:P], shut_rows[:, t, :], ident[:, :]
                                        ).then_inc(shut_turned, 1)
                with pe.Fori(0, ITERS) as k:
                    for h in range(SLOTS):
                        m = k * SLOTS + h
                        pe.wait_ge(scored, m + SLOTS - 1)
                        pe.wait_ge(onehotT_ready, m + 1)
                        for u, row in enumerate(load_rows(pe, m)):
                            last = nc.tensor.matmul(bank(h % 2)[:, u * P:(u + 1) * P],
                                                    onehotT[:, h % 2, u * P:(u + 1) * P],
                                                    acc_mem[:, bass.ds(row, D)], start=True, stop=True)
                        last.then_inc(q_ready, 1)
                        if h == 0:
                            pe.wait_ge(run_max, 3 * k + 3)
                            pe.wait_ge(shut, k + 1)
                            pe.wait_ge(stage_ready, 2 * k + 1)
                            nc.tensor.transpose(shut_now[:, 0:P], turn_stage, ident[:, :]).then_inc(scores_turned, 1)
                    pe.wait_ge(stage_ready, 2 * k + 2)
                    nc.tensor.transpose(bank(2)[:, 0:P], turn_stage, ident[:, :]).then_inc(scores_turned, 1)

            @block.vector
            def _(dve):
                did = [0]

                def step(ins):
                    did[0] += 1
                    ins.then_inc(prep, 1)
                    dve.wait_ge(prep, did[0])

                def make_onehotT(h, count):
                    dve.wait_ge(place_in[h % SLOTS], count)
                    nc.vector.tensor_scalar(onehotT[:, h % 2, :], placeT_bc[:, h % SLOTS, :], iota_col[:, :], None,
                                            ALU.is_equal).then_inc(onehotT_ready, 1)

                dve.wait_ge(dst_in, 32)
                nc.vector.memset(shut_rows[:, :, 0:1], -BIG)
                nc.vector.memset(reset[:, BLK:BLK + 1], -BIG)
                nc.vector.memset(shut_now[:, P:P + 1], -BIG)
                inner = shut_rows[:, :, 1:P]
                step(nc.vector.tensor_tensor(inner, dst_rows[:, :, 1:P], dst_rows[:, :, 0:P - 1], ALU.is_equal))
                nc.vector.tensor_scalar(inner, inner, BIG, -BIG, ALU.mult, ALU.add).then_inc(rows_ready, 1)
                firsts, lasts = (dst_rows[:, :, e:e + 1].rearrange("p t e -> p (t e)") for e in (0, P - 1))
                nc.vector.tensor_tensor(joins, firsts, before, ALU.is_equal)
                step(nc.vector.tensor_tensor(whole, firsts, lasts, ALU.is_equal))
                nc.vector.tensor_scalar(joins, joins, BIG, -BIG, ALU.mult, ALU.add)
                step(nc.vector.tensor_scalar(whole, whole, BIG, -BIG, ALU.mult, ALU.add))
                nc.vector.tensor_tensor(through, joins, whole, ALU.add).then_inc(joins_ready, 1)
                for t in range(TILES):
                    n = min(P, STEPS - t * P)
                    dve.wait_ge(shut_turned, t + 1)
                    nc.vector.tensor_copy(shut_T[:, t * P:t * P + n], bank(4 + t % 4)[:, 0:n]).then_inc(shut_kept, 1)
                places_T = place_T[:, 0:STEPS]
                step(nc.vector.tensor_scalar(outside, places_T, 0.0, None, ALU.is_ge))
                step(nc.vector.scalar_tensor_tensor(outside, places_T, float(P), outside, ALU.is_lt, ALU.mult))
                step(nc.vector.tensor_scalar(outside, outside, BIG, -BIG, ALU.mult, ALU.add))
                dve.sem_inc(q_ready, 1)
                dve.sem_inc(scored, SLOTS)
                dve.sem_inc(run_max, 3)
                dve.sem_inc(scores_turned, 1)
                dve.sem_inc(shut, 1)
                dve.wait_ge(joins_stored, 48)
                dve.wait_ge(shut_kept, TILES)

                def iteration(k, more):
                    for h in range(SLOTS):
                        m = k * SLOTS + h
                        if h == 0:
                            after(dve, run_max, 3 * k + 3, m_dve)
                            nc.vector.tensor_copy(
                                turn_stage.rearrange("p (h s) -> p h s", h=HEADS),
                                shut_T[:, bass.ds(k * ITER, ITER)].unsqueeze(1).to_broadcast([P, HEADS, ITER])
                            ).then_inc(stage_ready, 1)
                        if h == 2:
                            after(dve, scores_turned, 2 * k + 2, m_dve)
                            nc.vector.tensor_copy(reset[:, bass.ds(k * P, P)], shut_now[:, 0:P]).then_inc(shut, 1)
                        dve.wait_ge(q_ready, m + 1)
                        if h + 1 < SLOTS or more:
                            make_onehotT(h + 1, (k + 1 + (h + 1) // SLOTS) * 16)
                        dve.wait_ge(gathered[h], (k + 1) * (16 * GROUP))
                        dve.wait_ge(q_ready, m + 2)
                        product = kv_ring[:, h * GROUP:(h + 1) * GROUP, 0:D]
                        nc.vector.tensor_tensor(product, bank(h % 2).rearrange("p (u d) -> p u d", d=D), product,
                                                ALU.mult).then_inc(multiplied, 1)
                        after(dve, multiplied, m + 1, m_dve)
                        nc.vector.tensor_reduce(att_mem[:, bass.ds(m * GH, GH)].rearrange("p (u h) -> p u h", u=GROUP),
                                                product.rearrange("p u (h f) -> p u h f", f=DK), AX.X,
                                                ALU.add).then_inc(scored, 1)
                    dve.wait_ge(scored, (k + 2) * SLOTS)
                    att = att_mem[:, bass.ds(k * P, P)].rearrange("p (s h) -> p s h", h=HEADS)
                    nc.vector.tensor_tensor(
                        att, att, outside[:, bass.ds(k * ITER, ITER)].unsqueeze(2).to_broadcast([P, ITER, HEADS]),
                        ALU.add).then_inc(masked, 1)
                    after(dve, masked, k + 1, m_dve)
                    nc.vector.tensor_copy(turn_stage.rearrange("p (h s) -> p s h", h=HEADS), att
                                          ).then_inc(stage_ready, 1)
                    dve.wait_ge(shut, k + 2)
                    after(dve, scores_turned, 2 * k + 3, m_dve)
                    nc.vector.tensor_tensor_scan(turn_stage, reset[:, bass.ds(k * P, P)], bank(2)[:, 0:P], -BIG,
                                                 ALU.add, ALU.max).then_inc(run_max, 1)
                    dve.wait_ge(run_max, 3 * k + 4)
                    nc.vector.tensor_tensor_scan(both_ways[:, ::-1], shut_now[:, 1:P + 1][:, ::-1],
                                                 turn_stage[:, ::-1], -BIG, ALU.add, ALU.max).then_inc(run_max, 1)
                    after(dve, run_max, 3 * k + 5, m_dve)
                    nc.vector.tensor_copy(maxima[:, bass.ds(k * P, P)], both_ways).then_inc(run_max, 1)

                make_onehotT(0, 16)
                with dve.Fori(0, ITERS - 1) as k:
                    iteration(k, True)
                iteration(ITERS - 1, False)
        next_phase()

        BATCH = 4
        NB = ITERS
        BB = 5
        LOOPS, LEFT = NB // (BATCH * BB), NB % (BATCH * BB)
        assert LEFT == 1
        PER_BANK = ITER // 4
        carve = carver(acc_mem)
        joins8, whole8, through8 = carve(STEPS + 1, HEADS), carve(STEPS, HEADS), carve(STEPS, HEADS)
        carve = carver(ring_mem)
        into_next, into_before = carve(STEPS, HEADS), carve(STEPS, HEADS)
        from_before, from_next = through8, whole8
        stages = ring_mem[:, 0:BB * BATCH * P].rearrange("p (b c) -> p b c", b=BB)
        shut_stages = acc_mem[:, 2 * STEPS:2 * STEPS + BB * BATCH * P].rearrange("p (b c) -> p b c", b=BB)
        spread_w = P + ITER - 1
        spread = srctype_T[0:HEADS, 0:spread_w]
        rows_in, spread_iota, spread_ready = sem("rows_in_max"), sem("spread_iota"), sem("spread_ready")
        ends_psum, ends_ready, chain = sem("ends_psum"), sem("ends_ready"), sem("max_chain")
        shut_staged = sem("shut_staged")
        carries, carries_psum = sem("carries"), sem("carries_psum")
        fwd, staged, turned_back, shifted, weighed = (sem("fwd_max"), sem("max_staged"), sem("max_turned"),
                                                      sem("shifted"), sem("weighed"))
        with nc.Block() as block:
            @block.sync
            def _(sp):
                sp.dma_start(joins8, join_rows[0, 0:STEPS + 1].partition_broadcast(HEADS)).then_inc(rows_in, 16)
                sp.dma_start(whole8, join_rows[1, 0:STEPS].partition_broadcast(HEADS)).then_inc(rows_in, 16)
                sp.dma_start(through8, join_rows[2, 0:STEPS].partition_broadcast(HEADS)).then_inc(rows_in, 16)

            @block.gpsimd
            def _(pool):
                nc.gpsimd.iota(spread, [[1, spread_w]], base=1 - ITER, channel_multiplier=-ITER,
                               allow_small_or_imprecise_dtypes=True).then_inc(spread_iota, 1)

                def stage_shut(n_b, b, n):
                    after(pool, staged, n_b + 1, m_pool)
                    nc.gpsimd.tensor_copy(shut_stages[:, b, 0:n * P], reset[:, bass.ds(n_b * (BATCH * P) + 1, n * P)]
                                          ).then_inc(shut_staged, 1)

                pool.wait_ge(carries_psum, 2)
                pool.sem_inc(staged, BB)
                with pool.Fori(0, LOOPS) as i:
                    for b in range(BB):
                        stage_shut(i * BB + b, b, BATCH)
                stage_shut(LOOPS * BB, 0, LEFT)

            @block.tensor
            def _(pe):
                for way, column in enumerate((P - 1, 0)):
                    for t in range(ITER):
                        at = t % PER_BANK * NB
                        last = nc.tensor.matmul(bank(4 * way + t // PER_BANK)[0:HEADS, at:at + NB],
                                                ident[:, t::ITER], maxima[:, column::P], start=True, stop=True)
                    last.then_inc(ends_psum, 1)
                pe.wait_ge(spread_ready, 1)
                for way, row in enumerate((from_before, from_next)):
                    pe.wait_ge(carries, way + 1)
                    for t in range(ITER):
                        last = nc.tensor.matmul(bank(way)[:, 0:NB], spread[:, ITER - 1 - t:ITER - 1 - t + P],
                                                row[:, t::ITER], start=(t == 0), stop=(t == ITER - 1))
                    last.then_inc(carries_psum, 1)

                def turn_batch(n_b, b, n):
                    pe.wait_ge(shifted, n_b + 1)
                    pe.wait_ge(staged, n_b + 1 + BB)
                    for j in range(n):
                        last = nc.tensor.transpose(bank(b)[:, j * P:(j + 1) * P], stages[:, b, j * P:(j + 1) * P],
                                                   ident[:, :])
                    last.then_inc(turned_back, 1)

                with pe.Fori(0, LOOPS) as i:
                    for b in range(BB):
                        turn_batch(i * BB + b, b, BATCH)
                turn_batch(LOOPS * BB, 0, LEFT)

            @block.vector
            def _(dve):
                did = [0]

                def step(ins):
                    did[0] += 1
                    ins.then_inc(chain, 1)
                    dve.wait_ge(chain, did[0])

                def take_ends(row, banks):
                    for g in range(4):
                        last = nc.vector.tensor_copy(
                            row.rearrange("h (i t) -> h t i", t=ITER)[:, g * PER_BANK:(g + 1) * PER_BANK, :],
                            bank(banks + g)[0:HEADS, 0:PER_BANK * NB].rearrange("h (t i) -> h t i", i=NB))
                    step(last)

                dve.wait_ge(spread_iota, 1)
                nc.vector.tensor_scalar(spread, spread, 0.0, None, ALU.is_equal).then_inc(spread_ready, 1)
                dve.wait_ge(rows_in, 48)
                step(nc.vector.tensor_tensor(whole8, whole8, joins8[:, 1:STEPS + 1], ALU.add))
                dve.wait_ge(ends_psum, 1)
                take_ends(into_next, 0)
                step(nc.vector.tensor_tensor_scan(into_next, through8, into_next, -BIG, ALU.add, ALU.max))
                nc.vector.memset(from_before[:, 0:1], -BIG)
                nc.vector.tensor_tensor(from_before[:, 1:STEPS], into_next[:, 0:STEPS - 1], joins8[:, 1:STEPS],
                                        ALU.add).then_inc(carries, 1)
                dve.wait_ge(ends_ready, 1)
                step(nc.vector.tensor_tensor_scan(into_before[:, ::-1], whole8[:, ::-1], into_before[:, ::-1],
                                                  -BIG, ALU.add, ALU.max))
                nc.vector.memset(from_next[:, STEPS - 1:STEPS], -BIG)
                nc.vector.tensor_tensor(from_next[:, 0:STEPS - 1], into_before[:, 1:STEPS], joins8[:, 1:STEPS],
                                        ALU.add).then_inc(carries, 1)
                for way, column in enumerate((0, P - 1)):
                    dve.wait_ge(carries_psum, way + 1)
                    ends = maxima[:, column::P]
                    step(nc.vector.tensor_tensor(ends, ends, bank(way)[:, 0:NB], ALU.max))

                def stage_batch(n_b, b, n):
                    at = n_b * (BATCH * P)
                    stage, shut_after = stages[:, b, 0:n * P], shut_stages[:, b, 0:n * P]
                    after(dve, turned_back, n_b + 1, m_dve)
                    nc.vector.tensor_tensor_scan(stage, reset[:, bass.ds(at, n * P)], maxima[:, bass.ds(at, n * P)],
                                                 -BIG, ALU.add, ALU.max).then_inc(fwd, 1)
                    dve.wait_ge(shut_staged, n_b + 1)
                    dve.wait_ge(fwd, n_b + 1)
                    nc.vector.tensor_tensor_scan(stage[:, ::-1], shut_after[:, ::-1], stage[:, ::-1], -BIG, ALU.add,
                                                 ALU.max).then_inc(staged, 1)

                def shift_batch(n_b, b, n):
                    split = dict(b=n, t=ITER)
                    at = att_mem[:, bass.ds(n_b * (BATCH * P), n * P)].rearrange("p (b t h) -> p b h t", **split)
                    dve.wait_ge(turned_back, n_b + 1 + BB)
                    nc.vector.tensor_tensor(at, at, bank(b)[:, 0:n * P].rearrange("p (b h t) -> p b h t", **split),
                                            ALU.subtract).then_inc(shifted, 1)

                def iteration(i, more):
                    for b in range(BB):
                        if b + 1 < BB or more:
                            stage_batch(i * BB + b + 1, (b + 1) % BB, BATCH)
                        else:
                            stage_batch(LOOPS * BB, 0, LEFT)
                        shift_batch(i * BB + b, b, BATCH)

                dve.wait_ge(carries, 2)
                dve.sem_inc(turned_back, BB)
                dve.sem_inc(shifted, BB)
                stage_batch(0, 0, BATCH)
                with dve.Fori(0, LOOPS - 1) as i:
                    iteration(i, True)
                iteration(LOOPS - 1, False)
                shift_batch(LOOPS * BB, 0, LEFT)

            @block.scalar
            def _(act):
                act.wait_ge(ends_psum, 2)
                for g in range(4):
                    last = nc.scalar.activation(
                        into_before.rearrange("h (i t) -> h t i", t=ITER)[:, g * PER_BANK:(g + 1) * PER_BANK, :],
                        bank(4 + g)[0:HEADS, 0:PER_BANK * NB].rearrange("h (t i) -> h t i", i=NB), ACT.Copy)
                last.then_inc(ends_ready, 1)

                def exp_batch(n_b, n):
                    at = att_mem[:, bass.ds(n_b * (BATCH * P), n * P)]
                    after(act, shifted, n_b + 1 + BB, m_act)
                    nc.scalar.activation(at, at, ACT.Exp).then_inc(weighed, 1)

                with act.Fori(0, LOOPS) as i:
                    for b in range(BB):
                        exp_batch(i * BB + b, BATCH)
                exp_batch(LOOPS * BB, LEFT)
        next_phase()

        carve = carver(wide_mem)
        v_in_mem = carve(SLOTS * GROUP * D).rearrange("p (h u d) -> p h u d", h=SLOTS, u=GROUP)
        weighted = carve(2 * GROUP * AW).rearrange("p (b u c) -> p b u c", b=2, u=GROUP)
        odd_sums = carve(GROUP * AW).rearrange("p (b j c) -> p b j c", b=2, c=AW)
        acc_odd = carve(WINDOWS * AW)
        v_in = [sem(f"v_in{h}") for h in range(SLOTS)]
        v_used, values_ready, weights_ready = sem("v_used"), sem("values_ready"), sem("weights_ready")
        onehot_ready, groups_summed = sem("onehot_ready_v"), sem("groups_summed_v")
        added_even, added_odd, joined = sem("added_even"), sem("added_odd"), sem("joined")
        odd_copied = sem("odd_copied")
        PER = GROUP // 2
        part = lambda h, u: bank(2 * (h % 2) + u % 2)[:, u // 2 * 2 * D:u // 2 * 2 * D + AW]
        odd_part = lambda h: bank(2 * (h % 2) + 1).rearrange("p (j c) -> p j c", j=PER)[:, :, 0:AW]
        weights = lambda m: att_mem[:, bass.ds(m * GH, GH)].rearrange("p (u h) -> p u h", h=HEADS)
        with nc.Block() as block:
            @block.sync
            def _(sp):
                with sp.Fori(0, ITERS) as k:
                    for h in range(SLOTS):
                        m = k * SLOTS + h
                        sp.wait_ge(v_used, m + 1)
                        sp.dma_start(v_in_mem[:, h, :, :], v_rows[:, bass.ds(m * GROUP, GROUP), :]
                                     ).then_inc(v_in[h], 16)

            @block.gpsimd
            def _(pool):
                def multiply(m, h, loads):
                    after(pool, groups_summed, m + 1, m_pool)
                    after(pool, v_in[h % SLOTS], loads * 16, m_pool)
                    nc.gpsimd.tensor_tensor(
                        weighted[:, h % 2, :, 0:D].rearrange("p u (h f) -> p u h f", f=DK),
                        v_in_mem[:, h % SLOTS, :, :].rearrange("p u (h f) -> p u h f", f=DK),
                        weights(m).unsqueeze(3).to_broadcast([P, GROUP, HEADS, DK]), ALU.mult).then_inc(v_used, 1)

                def iteration(k, more):
                    for h in range(SLOTS):
                        m = k * SLOTS + h
                        if h + 1 < SLOTS or more:
                            multiply(m + 1, h + 1, k + 1 + (h + 1) // SLOTS)
                        rows = load_rows(pool, m)
                        after(pool, odd_copied, m + 3, m_pool)
                        for j, u in enumerate(range(1, GROUP, 2)):
                            row = acc_odd[:, bass.ds(rows[u], AW)]
                            after(pool, added_odd, m * PER + j + 2 * PER, m_pool)
                            nc.gpsimd.tensor_tensor(row, row, odd_sums[:, h % 2, j, :], ALU.add).then_inc(added_odd, 1)

                pool.sem_inc(v_used, SLOTS)
                pool.sem_inc(added_odd, 2 * PER - 1)
                nc.gpsimd.memset(acc_odd, 0.0).then_inc(added_odd, 1)
                multiply(0, 0, 1)
                with pool.Fori(0, ITERS - 1) as k:
                    iteration(k, True)
                iteration(ITERS - 1, False)

            @block.scalar
            def _(act):
                def copy_weights(m, h):
                    after(act, groups_summed, m + 1, m_act)
                    nc.scalar.activation(weighted[:, h % 2, :, D:AW], weights(m), ACT.Copy
                                         ).then_inc(weights_ready, 1)

                def iteration(k, more):
                    for h in range(SLOTS):
                        m = k * SLOTS + h
                        if h + 1 < SLOTS or more:
                            copy_weights(m + 1, h + 1)
                        act.wait_ge(added_odd, m * PER + PER)
                        act.wait_ge(groups_summed, m + 3)
                        nc.scalar.activation(odd_sums[:, h % 2, :, :], odd_part(h), ACT.Copy
                                             ).then_inc(odd_copied, 1)

                act.sem_inc(odd_copied, 2)
                copy_weights(0, 0)
                with act.Fori(0, ITERS - 1) as k:
                    iteration(k, True)
                iteration(ITERS - 1, False)

            @block.tensor
            def _(pe):
                pe.sem_inc(groups_summed, 2)
                with pe.Fori(0, ITERS) as k:
                    for h in range(SLOTS):
                        m = k * SLOTS + h
                        pe.wait_ge(onehot_ready, m + 1)
                        pe.wait_ge(added_even, m * PER + PER)
                        pe.wait_ge(odd_copied, m + 1)
                        pe.wait_ge(weights_ready, m + 1)
                        pe.wait_ge(v_used, m + 1 + SLOTS)
                        for u in range(GROUP):
                            last = nc.tensor.matmul(part(h, u), onehot[:, h % 2, u, :],
                                                    weighted[:, h % 2, u, :], start=True, stop=True)
                        last.then_inc(groups_summed, 1)

            @block.vector
            def _(dve):
                def make_onehot(m, h):
                    nc.vector.tensor_tensor(
                        onehot[:, h % 2, :, :],
                        place_T[:, bass.ds(m * GROUP, GROUP)].unsqueeze(2).to_broadcast([P, GROUP, P]),
                        iota_row[:, :].unsqueeze(1).to_broadcast([P, GROUP, P]),
                        ALU.is_equal).then_inc(onehot_ready, 1)

                dve.sem_inc(added_even, 2 * PER - 1)
                nc.vector.memset(acc_mem[:, :], 0.0).then_inc(added_even, 1)
                make_onehot(0, 0)
                with dve.Fori(0, ITERS) as k:
                    for h in range(SLOTS):
                        m = k * SLOTS + h
                        dve.wait_ge(groups_summed, m + 2)
                        make_onehot(m + 1, h + 1)
                        rows = load_rows(dve, m)
                        dve.wait_ge(groups_summed, m + 3)
                        for j, u in enumerate(range(0, GROUP, 2)):
                            row = acc_mem[:, bass.ds(rows[u], AW)]
                            dve.wait_ge(added_even, m * PER + j + 2 * PER)
                            nc.vector.tensor_tensor(row, row, part(h, u), ALU.add).then_inc(added_even, 1)
                dve.wait_ge(added_odd, ITERS * SLOTS * PER + 2 * PER)
                dve.wait_ge(added_even, ITERS * SLOTS * PER + 2 * PER)
                nc.vector.tensor_tensor(acc_mem[:, :], acc_mem[:, :], acc_odd, ALU.add).then_inc(joined, 1)
        next_phase()

        types_f32 = att_mem[:, 0:WINDOWS * P]
        types_int = types_f32.bitcast(i32)
        x1 = wide_mem[:, 0:WINDOWS * D].rearrange("p (w d) -> p w d", d=D)
        res = wide_mem[:, WINDOWS * D:2 * WINDOWS * D].rearrange("p (w d) -> p w d", d=D)
        carve = carver(att_mem, WINDOWS * P)
        w_a = carve(TYPES * D).rearrange("p (t o) -> p t o", t=TYPES)
        b_a = carve(D, TYPES)
        gain_shift = carve(2 * D, TYPES)
        gate_of_type = carve(TYPES)
        type_col = carve(WINDOWS)
        gate, keep, mean2, rstd2, spare_col = (carve(WINDOWS) for _ in range(5))
        rden = carve(WINDOWS * HEADS).rearrange("p (w h) -> p w h", h=HEADS)
        normal = carve(2 * 4 * P).rearrange("p (b c) -> p b c", b=2)
        carve = carver(ring_mem)
        gelu = onehot[:, :, :, :].rearrange("p b u c -> p b (u c)")
        g_typed = carve(TYPES * 4 * P).rearrange("p (t c) -> p t c", t=TYPES)
        is_type2 = carve(2 * 4 * P, TYPES).rearrange("p (b c) -> p b c", b=2)
        gated = carve(4 * P)
        w_in, types_in, cols_in, rows_in = sem("out_w_in"), sem("types2_in"), sem("type_col_in"), sem("rows_in")
        zeroed, prep, sig = sem("cols_zero"), sem("prep"), sem("gate_sigmoid")
        normed, gelued, gT, g_typed_ready = sem("normed"), sem("gelued"), sem("gT"), sem("g_typed")
        products_ready, res_ready, gated_s = sem("out_product"), sem("res_ready"), sem("gated")
        type_col_i = type_col.bitcast(i32)
        with nc.Block() as block:
            @block.sync
            def _(sp):
                sp.dma_start(types_int[:, 0:N], a["node_type_3"].partition_broadcast(P)).then_inc(types_in, 16)
                sp.dma_start(w_a, a["L1_gnn_Wa"].rearrange("t i o -> i t o")).then_inc(w_in, 16)
                sp.dma_start(b_a, a["L1_gnn_ba"]).then_inc(w_in, 16)
                sp.dma_start(gain_shift[:, 0:D], a["L1_gnn_ln_g"]).then_inc(w_in, 16)
                sp.dma_start(gain_shift[:, D:2 * D], a["L1_gnn_ln_b"]).then_inc(w_in, 16)
                sp.dma_start(gate_of_type, a["L1_gnn_skip"].partition_broadcast(P)).then_inc(w_in, 16)
                sp.wait_ge(zeroed, 1)
                types_1d = a["node_type_3"]
                sp.dma_start(type_col_i[:, 0:WINDOWS - 1],
                             types_1d[0:(WINDOWS - 1) * P].rearrange("(w p) -> p w", p=P),
                             allow_slow_non_contiguous=True).then_inc(cols_in, 16)
                sp.dma_start(type_col_i[0:TAIL, WINDOWS - 1:WINDOWS],
                             types_1d[(WINDOWS - 1) * P:N].rearrange("(p o) -> p o", o=1)).then_inc(cols_in, 16)
                sp.dma_start(res, hin_rows.rearrange("(w p) d -> p w d", p=P)).then_inc(rows_in, 16)
                sp.dma_start(x1, x1_rows.rearrange("(w p) d -> p w d", p=P)).then_inc(rows_in, 16)
                sp.wait_ge(rows_in, 32)

            @block.vector
            def _(dve):
                n_prep = [0]

                def step(ins):
                    n_prep[0] += 1
                    ins.then_inc(prep, 1)
                    dve.wait_ge(prep, n_prep[0])

                nc.vector.memset(types_int[:, N:WINDOWS * P], 0)
                nc.vector.memset(type_col_i, 0).then_inc(zeroed, 1)
                step(nc.vector.tensor_scalar(rden, acc[:, :, D:AW], 1e-16, None, ALU.add))
                step(nc.vector.reciprocal(rden, rden))
                dve.wait_ge(zeroed, 1)
                dve.wait_ge(types_in, 16)
                step(nc.vector.tensor_copy(types_f32, types_int))
                dve.wait_ge(cols_in, 32)
                step(nc.vector.tensor_copy(type_col, type_col_i))
                dve.wait_ge(sig, 1)
                step(nc.vector.memset(gate, 0.0))
                for t in range(TYPES):
                    step(nc.vector.tensor_scalar(spare_col, type_col, float(t), gate_of_type[:, t:t + 1],
                                                 ALU.is_equal, ALU.mult))
                    step(nc.vector.tensor_tensor(gate, gate, spare_col, ALU.add))
                step(nc.vector.tensor_scalar(keep, gate, -1.0, 1.0, ALU.mult, ALU.add))
                dve.wait_ge(rows_in, 32)
                step(nc.vector.tensor_tensor(res, res, keep.unsqueeze(2).to_broadcast([P, WINDOWS, D]), ALU.mult))

                with dve.Fori(0, WB) as i:
                    for b, (first, n) in enumerate(HALVES):
                        w = i * BODY + first
                        nc.vector.tensor_tensor(
                            normal[:, b, 0:n * P].rearrange("p (w h f) -> p w h f", h=HEADS, f=DK),
                            acc[:, bass.ds(w, n), 0:D].rearrange("p w (h f) -> p w h f", f=DK),
                            rden[:, bass.ds(w, n), :].unsqueeze(3).to_broadcast([P, n, HEADS, DK]),
                            ALU.mult).then_inc(normed, 1)
                    for b, (first, n) in enumerate(HALVES):
                        q = i * 2 + b
                        w = i * BODY + first
                        dve.wait_ge(gT, q + 1)
                        dve.wait_ge(products_ready, q + 1)
                        for t in range(TYPES):
                            nc.vector.scalar_tensor_tensor(
                                g_typed[:, t, 0:n * P], types_f32[:, bass.ds(w * P, n * P)], float(t),
                                bank(b)[:, 0:n * P], ALU.is_equal, ALU.mult)
                        nc.vector.tensor_scalar(is_type2[:, b, 0:n * P], types_f32[0:TYPES, bass.ds(w * P, n * P)],
                                                iota_col[0:TYPES, :], None, ALU.is_equal).then_inc(g_typed_ready, 1)
                        dve.wait_ge(products_ready, q + 2)
                        nc.vector.tensor_tensor(
                            gated[:, 0:n * P].rearrange("p (w d) -> p w d", d=D),
                            bank(2 + b)[:, 0:n * P].rearrange("p (w d) -> p w d", d=D),
                            gate[:, bass.ds(w, n)].unsqueeze(2).to_broadcast([P, n, D]), ALU.mult
                        ).then_inc(gated_s, 1)
                        dve.wait_ge(gated_s, q + 1)
                        nc.vector.tensor_tensor(windows(res, w, n), windows(res, w, n), gated[:, 0:n * P], ALU.add
                                                ).then_inc(res_ready, 1)

            @block.scalar
            def _(act):
                act.wait_ge(w_in, 5 * 16)
                nc.scalar.activation(gate_of_type, gate_of_type, ACT.Sigmoid).then_inc(sig, 1)
                with act.Fori(0, WB) as i:
                    for b, (first, n) in enumerate(HALVES):
                        act.wait_ge(normed, i * 2 + b + 1)
                        nc.scalar.activation(gelu[:, b, 0:n * P], normal[:, b, 0:n * P], ACT.Gelu
                                             ).then_inc(gelued, 1)

            @block.tensor
            def _(pe):
                pe.wait_ge(w_in, 5 * 16)
                pe.sem_inc(products_ready, 1)
                with pe.Fori(0, WB) as i:
                    for b, (first, n) in enumerate(HALVES):
                        pe.wait_ge(gelued, i * 2 + b + 1)
                        for j in range(n):
                            last = nc.tensor.transpose(bank(b)[:, j * P:(j + 1) * P], gelu[:, b, j * P:(j + 1) * P],
                                                       ident[:, :])
                        last.then_inc(gT, 1)
                    for b, (first, n) in enumerate(HALVES):
                        q = i * 2 + b
                        pe.wait_ge(g_typed_ready, q + 1)
                        for j in range(n):
                            at = slice(j * P, (j + 1) * P)
                            for t in range(TYPES):
                                nc.tensor.matmul(bank(2 + b)[:, at], g_typed[:, t, at], w_a[:, t, :],
                                                 start=(t == 0), stop=False)
                            last = nc.tensor.matmul(bank(2 + b)[:, at], is_type2[:, b, at], b_a,
                                                    start=False, stop=True)
                        last.then_inc(products_ready, 1)
        next_phase()

        chain, squared, rooted = sem("out_chain"), sem("out_squared"), sem("out_rooted")
        affine, affine_used, typed2, done = sem("affine"), sem("affine_used"), sem("typed_rows"), sem("out_done")
        piece, out_stored = sem("piece"), sem("out_stored")
        centred = acc_mem[:, 0:WINDOWS * D].rearrange("p (w d) -> p w d", d=D)
        square = res
        bc = lambda v: v.unsqueeze(2).to_broadcast([P, WINDOWS, D])
        with nc.Block() as block:
            @block.vector
            def _(dve):
                def step(ins, n):
                    ins.then_inc(chain, 1)
                    dve.wait_ge(chain, n)

                step(nc.vector.tensor_reduce(mean2, res, AX.X, ALU.add), 1)
                step(nc.vector.tensor_scalar(mean2, mean2, 1.0 / D, None, ALU.mult), 2)
                step(nc.vector.tensor_tensor(centred, res, bc(mean2), ALU.subtract), 3)
                dve.wait_ge(squared, 1)
                step(nc.vector.tensor_reduce(rstd2, square, AX.X, ALU.add), 4)
                step(nc.vector.tensor_scalar(rstd2, rstd2, 1.0 / D, EPS, ALU.mult, ALU.add), 5)
                dve.wait_ge(rooted, 1)
                step(nc.vector.reciprocal(rstd2, rstd2), 6)
                with dve.Fori(0, WB) as i:
                    for b, (first, n) in enumerate(HALVES):
                        q = i * 2 + b
                        w = i * BODY + first
                        dve.wait_ge(affine, q + 1)
                        nc.vector.tensor_scalar(is_type2[:, b, 0:n * P], types_f32[0:TYPES, bass.ds(w * P, n * P)],
                                                iota_col[0:TYPES, :], None, ALU.is_equal).then_inc(typed2, 1)
                        rows = centred[:, bass.ds(w, n), :]
                        nc.vector.tensor_tensor(rows, rows, rstd2[:, bass.ds(w, n)].unsqueeze(2).to_broadcast(
                            [P, n, D]), ALU.mult).then_inc(piece, 1)
                        dve.wait_ge(affine, q + 3)
                        dve.wait_ge(piece, 3 * q + 1)
                        flat = rows.rearrange("p w d -> p (w d)")
                        nc.vector.tensor_tensor(flat, flat, bank(2 * b)[:, 0:n * P], ALU.mult).then_inc(piece, 1)
                        dve.wait_ge(piece, 3 * q + 2)
                        nc.vector.tensor_tensor(flat, flat, bank(2 * b + 1)[:, 0:n * P], ALU.add
                                                ).then_inc(piece, 1)
                        dve.wait_ge(piece, 3 * q + 3)
                        nc.vector.tensor_tensor(flat, flat, windows(x1, w, n), ALU.add).then_inc(done, 1)

            @block.scalar
            def _(act):
                act.wait_ge(chain, 3)
                nc.scalar.activation(square, centred, ACT.Square).then_inc(squared, 1)
                act.wait_ge(chain, 5)
                nc.scalar.activation(rstd2, rstd2, ACT.Sqrt).then_inc(rooted, 1)

            @block.tensor
            def _(pe):
                pe.sem_inc(affine, 2)
                pe.sem_inc(done, 2)
                with pe.Fori(0, WB) as i:
                    for b, (first, n) in enumerate(HALVES):
                        q = i * 2 + b
                        pe.wait_ge(done, q + 1)
                        pe.wait_ge(typed2, q + 1)
                        for j in range(n):
                            at = slice(j * P, (j + 1) * P)
                            for c in range(2):
                                last = nc.tensor.matmul(bank(2 * b + c)[:, at], is_type2[:, b, at],
                                                        gain_shift[:, c * D:(c + 1) * D], start=True, stop=True)
                        last.then_inc(affine, 1)

            @block.sync
            def _(sp):
                body = out[0:(WINDOWS - 1) * P, :].rearrange("(w p) d -> p w d", p=P)
                with sp.Fori(0, WB - 1) as i:
                    sp.wait_ge(done, (i + 1) * 2 + 2)
                    sp.dma_start(body[:, bass.ds(i * BODY, BODY), :], centred[:, bass.ds(i * BODY, BODY), :]
                                 ).then_inc(out_stored, 16)
                sp.wait_ge(done, WB * 2 + 2)
                sp.dma_start(body[:, WINDOWS - BODY:WINDOWS - 1, :], centred[:, WINDOWS - BODY:WINDOWS - 1, :]
                             ).then_inc(out_stored, 16)
                sp.dma_start(out[(WINDOWS - 1) * P:N, :], centred[0:TAIL, WINDOWS - 1, :]).then_inc(out_stored, 16)
                sp.wait_ge(out_stored, 16 * (WB + 1))


def kernel(**inputs):
    import numpy as np
    import concourse.bacc as bacc
    from concourse.bass_utils import run_bass_kernel_spmd

    nc = bacc.Bacc("TRN2", target_bir_lowering=False, num_devices=1)
    arrays, args = {}, {}
    for name, value in inputs.items():
        array = np.ascontiguousarray(value)
        arrays[f"in_{name}"] = array
        args[name] = nc.dram_tensor(f"in_{name}", array.shape, mybir.dt.from_np(array.dtype),
                                    kind="ExternalInput").ap()
    shape = inputs["x"].shape
    out = nc.dram_tensor("out_x", shape, mybir.dt.float32, kind="ExternalOutput").ap()
    gnn_kernel(nc, args, out)
    result = run_bass_kernel_spmd(nc, [arrays], core_ids=[0])
    return result.results[0]["out_x"]
```
